# Optimizing a Trainium2 kernel written in Bass

```python
import numpy as np
import jax
import jax.numpy as jnp

def _softmax(x, axis=-1):
    return jax.nn.softmax(x, axis=axis)

def _gelu(x):
    return jax.nn.gelu(x, approximate=True)

def _silu(x):
    return jax.nn.silu(x)

def _sigmoid(x):
    return jax.nn.sigmoid(x)

def _layernorm(x, axis=-1, eps=1e-05):
    m = jnp.mean(x, axis=axis, keepdims=True)
    v = jnp.var(x, axis=axis, keepdims=True)
    return (x - m) / jnp.sqrt(v + eps)

def _scatter_add(tgt, idx, src, axis=0):
    return tgt.at[idx].add(src)

def _segment_sum(src, seg, n):
    return jax.ops.segment_sum(src, seg, n)
kernel_name = 'mk_seq_postln_d1_jaxref_r4_c802eb'

def setup_inputs(seed: int=0):
    np.random.seed(seed)
    _w = jnp.asarray

    def _L0_attn_setup():
        import jax, jax.numpy as jnp
        import numpy as np
        import math
        D_MODEL = 512
        NUM_HEADS = 16
        HEAD_DIM = D_MODEL // NUM_HEADS
        key = jax.random.key(seed)
        k_x, k_wqkv, k_bqkv, k_wo, k_bo = jax.random.split(key, 5)
        B, S = (2, 512)
        scale = 1.0 / math.sqrt(D_MODEL)
        return {'x': jax.random.normal(k_x, (B, S, D_MODEL), dtype=jnp.float32), 'w_qkv': jax.random.normal(k_wqkv, (3 * D_MODEL, D_MODEL), dtype=jnp.float32) * scale, 'b_qkv': jax.random.normal(k_bqkv, (3 * D_MODEL,), dtype=jnp.float32) * 0.01, 'w_out': jax.random.normal(k_wo, (D_MODEL, D_MODEL), dtype=jnp.float32) * scale, 'b_out': jax.random.normal(k_bo, (D_MODEL,), dtype=jnp.float32) * 0.01}
    _L0_attn_in = _L0_attn_setup()

    def _L0_ffn_setup():
        import jax, jax.numpy as jnp
        import numpy as np

        @jax.custom_vjp
        def ste_sign(x):
            return jnp.sign(x)

        def _ste_fwd(x):
            return (jnp.sign(x), None)

        def _ste_bwd(_, g):
            return (g,)
        ste_sign.defvjp(_ste_fwd, _ste_bwd)
        D_MODEL = 512
        D_HIDDEN = 2048
        key = jax.random.key(seed)
        k_x, k_up, k_dn = jax.random.split(key, 3)
        x = jax.random.normal(k_x, (2, 512, D_MODEL), dtype=jnp.float32)
        up_weight = jax.random.normal(k_up, (D_HIDDEN, D_MODEL), dtype=jnp.float32) * 0.02
        down_weight = jax.random.normal(k_dn, (D_MODEL, D_HIDDEN), dtype=jnp.float32) * 0.02
        up_scale = jnp.ones((D_HIDDEN,), dtype=jnp.float32)
        down_scale = jnp.ones((D_MODEL,), dtype=jnp.float32)
        output_scale = jnp.ones((1,), dtype=jnp.float32)
        return {'x': x, 'up_weight': up_weight, 'down_weight': down_weight, 'up_scale': up_scale, 'down_scale': down_scale, 'output_scale': output_scale}
    _L0_ffn_in = _L0_ffn_setup()
    _d = {'L0_attn_x': _L0_attn_in['x'], 'L0_attn_w_qkv': _L0_attn_in['w_qkv'], 'L0_attn_b_qkv': _L0_attn_in['b_qkv'], 'L0_attn_w_out': _L0_attn_in['w_out'], 'L0_attn_b_out': _L0_attn_in['b_out'], 'L0_ffn_up_weight': _L0_ffn_in['up_weight'], 'L0_ffn_down_weight': _L0_ffn_in['down_weight'], 'L0_ffn_up_scale': _L0_ffn_in['up_scale'], 'L0_ffn_down_scale': _L0_ffn_in['down_scale'], 'L0_ffn_output_scale': _L0_ffn_in['output_scale']}
    _x0 = _d['L0_attn_x']
    _d['L0_attn_x'] = jax.random.normal(jax.random.fold_in(jax.random.key(seed), 1), (2, 1024, 512), dtype=_x0.dtype)
    del _x0
    return _d

def reference(L0_attn_x, L0_attn_w_qkv, L0_attn_b_qkv, L0_attn_w_out, L0_attn_b_out, L0_ffn_up_weight, L0_ffn_down_weight, L0_ffn_up_scale, L0_ffn_down_scale, L0_ffn_output_scale):

    def _L0_attn_ref(x, w_qkv, b_qkv, w_out, b_out):
        import jax, jax.numpy as jnp
        import numpy as np
        import math
        D_MODEL = 512
        NUM_HEADS = 16
        HEAD_DIM = D_MODEL // NUM_HEADS
        B, S, D = x.shape
        H, Hd = (NUM_HEADS, HEAD_DIM)
        qkv = jnp.einsum('bsd,ed->bse', x, w_qkv) + b_qkv
        qkv = qkv.reshape(B, S, 3, H, Hd)
        q = jnp.transpose(qkv[:, :, 0], (0, 2, 1, 3))
        k = jnp.transpose(qkv[:, :, 1], (0, 2, 1, 3))
        v = jnp.transpose(qkv[:, :, 2], (0, 2, 1, 3))
        scores = jnp.einsum('bhqd,bhkd->bhqk', q, k) / math.sqrt(Hd)
        causal = jnp.triu(jnp.full((S, S), -jnp.inf, dtype=scores.dtype), k=1)
        scores = scores + causal[None, None]
        attn = jax.nn.softmax(scores, axis=-1)
        out = jnp.einsum('bhqk,bhkd->bhqd', attn, v)
        out = jnp.transpose(out, (0, 2, 1, 3)).reshape(B, S, D)
        return jnp.einsum('bsd,ed->bse', out, w_out) + b_out

    def _L0_ffn_ref(x, up_weight, down_weight, up_scale, down_scale, output_scale):
        import jax, jax.numpy as jnp
        import numpy as np

        @jax.custom_vjp
        def ste_sign(x):
            return jnp.sign(x)

        def _ste_fwd(x):
            return (jnp.sign(x), None)

        def _ste_bwd(_, g):
            return (g,)
        ste_sign.defvjp(_ste_fwd, _ste_bwd)
        D_MODEL = 512
        D_HIDDEN = 2048
        up_w = ste_sign(up_weight)
        down_w = ste_sign(down_weight)
        hidden = jnp.einsum('bsd,hd->bsh', x, up_w) * up_scale
        hidden = jax.nn.relu(hidden)
        out = jnp.einsum('bsh,dh->bsd', hidden, down_w) * down_scale
        return out * output_scale
    x = L0_attn_x
    x = _layernorm(x + _L0_attn_ref(x, L0_attn_w_qkv, L0_attn_b_qkv, L0_attn_w_out, L0_attn_b_out), axis=-1)
    x = _layernorm(x + _L0_ffn_ref(x, L0_ffn_up_weight, L0_ffn_down_weight, L0_ffn_up_scale, L0_ffn_down_scale, L0_ffn_output_scale), axis=-1)
    return x

_drawn_inputs = setup_inputs


def setup_inputs(seed=0):
    import zlib

    import numpy as np

    out = dict(_drawn_inputs(seed))
    spreads = {'L0_ffn_up_scale': (1.0, 0.2), 'L0_ffn_down_scale': (1.0, 0.2)}
    factors = {'L0_attn_b_qkv': 6.112, 'L0_attn_b_out': 6.961}
    for name, (base, spread) in spreads.items():
        noise = np.random.default_rng([zlib.crc32(name.encode()), seed]).standard_normal(out[name].shape)
        drawn = base * np.exp(spread * noise) if base else spread * noise
        out[name] = jnp.asarray(drawn.astype(out[name].dtype))
    for name, factor in factors.items():
        out[name] = (out[name] * factor).astype(out[name].dtype)
    return out
```

```python
import numpy as np
import concourse.bass as bass
from concourse import mybir
from contextlib import ExitStack

FP32 = mybir.dt.float32
FP32R = mybir.dt.float32r
BF16 = mybir.dt.bfloat16
ALU = mybir.AluOpType
ACT = mybir.ActivationFunctionType
AXIS_X = mybir.AxisListType.X

P = 128
BATCH, SEQ, D, HEADS, FF = 2, 1024, 512, 16, 2048
HD = D // HEADS
TOKENS = BATCH * SEQ
DC = D // P
GROUPS = D // P
GH = P // HD
HALF = 512
NHALF = SEQ // HALF
QT = SEQ // P
STEPS = BATCH * GROUPS
SCALE = float(HD) ** -0.5
NEG = -3.0e38
EPS = 1e-5

PIECES = [(f, j, h) for f in range(NHALF) for j in range(4 * (f + 1)) for h in range(GH)]
NP = len(PIECES)
RING = 8
DIAG = [n for n, (f, j, h) in enumerate(PIECES) if j >= 4 * f]
ND = len(DIAG)
UNITS = [(h, i, c) for h in range(GH) for i in range(QT) for c in range(i // 4 + 1)]
NU = len(UNITS)
NC_ = 6
PROJ = [(0, 0), (1, 0), (0, 1), (1, 1), (2, 0), (2, 1)]
PARTS = [(0, 0), (1, 0), (0, 1)]
NJOBS = 9
CH = TOKENS // HALF
TT = HALF // P
HM = FF // P


class Multiples:

    def __init__(self, eng, i):
        self.eng, self.i, self.kept = eng, i, {}

    def __call__(self, k):
        if isinstance(self.i, int) or k == 1:
            return self.i * k
        if k not in self.kept:
            self.kept[k] = self.eng.snap(self.i * k)
        return self.kept[k]


class Step:

    def __init__(self, g, off):
        self.g, self.off, self.slot = g, off, off % 2
        self.batch, self.group = off % 2, g(1) + off // 2
        self.leading = isinstance(g(1), int) and g(1) == 0

    def count(self, per, more=0):
        return self.g(2 * per) + (self.off * per + more)


def wait(eng, sem, value):
    if not isinstance(value, int) or value > 0:
        eng.wait_ge(sem, value)


def piece_cols(n):
    f, j, _ = PIECES[n]
    lo = max(HALF * f, P * j)
    return lo, HALF * (f + 1) - lo, lo - HALF * f


def pv_slot(n):
    return n + 4 if PIECES[n][0] == 0 else n + 7


SLOTS = pv_slot(NP - 1) + 1


def plan(attend, maxima, project, prep=0, lead=False):
    at = [[] for _ in range(SLOTS)]
    if attend:
        for n in range(NP):
            at[n].append(("score", n))
            at[pv_slot(n)].append(("pv", n))
        at[pv_slot(15) + 1].append(("norm", 0))
        at[SLOTS - 1].append(("norm", 1))
    if maxima:
        at[0].append(("stack", 0))
        at[0].append(("vturn", 0))
        at[3].append(("vturn", 1))
        for u in range(NU):
            at[9 + u * 35 // NU].append(("max", u))
        at[45].append(("shift", 0))
    if project:
        at[0].insert(0, ("weights", 0))
        first, width = (8, 6.6)
        for k in range(NC_):
            for m in range(12):
                at[int(first + width * k + m * 0.42)].append(("proj", 12 * k + m))
            at[int(first + width * k + 11 * 0.42)].append(("spill", k))
    if lead:
        for n in range(2 * DC):
            at[12 + 4 * n].append(("second_x", n))
    if prep:
        for k in (range(0, 4) if prep == 1 else range(4, NJOBS)):
            s = 8 * k + 8 if prep == 1 else 8 * (k - 4)
            at[s].append(("job", k))
            for q in range(4):
                at[s + 6 + 2 * q].append(("sign", 4 * k + q))
    return [x for slot in at for x in slot]


def build(nc, x_rows, x_cols, w_qkv, b_qkv, w_out, b_out, up_w, down_w, up_s, down_s, out_s, out):
    top = ExitStack()
    with top:
        def sem(name):
            return top.enter_context(nc.semaphore(name))

        def sb(ctx, name, shape, dt, side=None):
            return ctx.enter_context(nc.sbuf_tensor(name, shape, dt, side=side))

        def pb(ctx, name, shape):
            return ctx.enter_context(nc.psum_tensor(name, shape, FP32))

        heads_dram = nc.dram_tensor("heads_t", [GROUPS, P, TOKENS], FP32, kind="Internal").ap()

        s_const = sem("consts_ready")
        s_passed = sem("register_wait_passed")
        s_x = [sem(f"x_loaded{i}") for i in range(RING)]
        s_xh = sem("x_high_ready")
        s_xl = sem("x_low_ready")
        s_xlp = sem("x_low_ready_pool")
        s_wd = sem("w_group_loaded")
        s_bias = sem("bias_loaded")
        s_wh = sem("w_high_ready")
        s_wl = sem("w_low_ready")
        s_proj = sem("projection_done")
        s_spill = sem("projection_copied")
        s_lo = sem("qk_low_ready")
        s_stack = [sem(f"stack_filled{h}") for h in range(GH)]
        s_vt = sem("v_turned")
        s_vc = sem("v_ready")
        s_unit = sem("unit_scores_ready")
        s_max = sem("unit_max_ready")
        s_mc = sem("row_max_ready")
        s_mt = sem("row_max_turned")
        s_mh = sem("shift_high_ready")
        s_ml = sem("shift_low_ready")
        s_md = sem("shift_rows_filled")
        s_score = sem("scores_ready")
        s_exp = sem("probs_ready")
        s_mask = sem("probs_masked")
        s_pv = sem("probs_used")
        s_rc = sem("row_sum_inverted")
        s_norm = sem("heads_normalized")
        s_st = [sem(f"heads_stored{f}") for f in range(NHALF)]
        s_raw = [sem(f"raw_weights_loaded{i}") for i in range(2)]
        s_sign = sem("late_weights_ready")
        s_wol = sem("w_out_low_ready")

        left, right = ExitStack(), ExitStack()
        q_stack = sb(left, "q_stack", [P, 2, GH, SEQ], FP32R)
        k_stack = sb(left, "k_stack", [P, 2, GH, SEQ], FP32R)
        v_cols = sb(left, "v_cols", [P, 2, SEQ], FP32)
        v_rows = sb(left, "v_rows", [P, 2, QT, P], FP32)
        probs = sb(left, "probs", [P, RING, HALF], FP32)
        inv_sum = sb(left, "inv_sum", [P, HALF], FP32)
        heads_sb = sb(left, "heads_sb", [P, NHALF, HALF], FP32)
        causal = sb(left, "causal", [P, HALF], BF16)
        ident = sb(left, "ident", [P, P], FP32)
        ones = sb(left, "ones", [P, HD], FP32)
        maxes = sb(left, "maxes", [P, 2, GH * QT], FP32)
        row_max = sb(left, "row_max", [P, GH * QT], FP32)
        shift_h = sb(left, "shift_h", [GH * QT, P], FP32R)
        shift_l = sb(left, "shift_l", [GH * QT, P], FP32R)
        bias_sb = sb(left, "bias_sb", [P, GROUPS, 3], FP32)
        bias_g = sb(left, "bias_g", [P, 2, 3], FP32)

        xs = [sb(right, f"x_{n}", [P, DC, TOKENS], FP32R, "right") for n in ("high", "low")]
        w_raw = sb(right, "w_raw", [P, DC, 3, P], FP32, "right")
        ws = [sb(right, f"w_{n}", [P, DC, 3, P], FP32R, "right") for n in ("high", "low")]
        qk_h = sb(right, "qk_h", [P, 2, SEQ], FP32R, "right")
        qk_l = sb(right, "qk_l", [P, 2, SEQ], FP32R, "right")
        qk_full = sb(right, "qk_full", [P, HALF], FP32, "right")

        pa = ExitStack()
        ps_proj = pb(pa, "ps_proj", [P, HALF])
        ps_turn = pb(pa, "ps_turn", [P, HALF])
        ps_unit = [pb(pa, f"ps_unit{i}", [P, HALF]) for i in range(2)]
        ps_score = [pb(pa, f"ps_score{i}", [P, HALF]) for i in range(2)]
        ps_heads = pb(pa, "ps_heads", [P, HALF])
        ps_sum = pb(pa, "ps_sum", [P, HALF])

        def raw_piece(b, n):
            f, c = n // DC, n % DC
            return c, b * SEQ + f * HALF, probs[:, n, :]

        x_side, attn_side = right, left
        x_side.close()
        late = top.enter_context(ExitStack())
        up_sb = sb(late, "up_sb", [P, HM, DC, P], FP32R, "right")
        down_sb = sb(late, "down_sb", [P, HM, D], FP32R, "right")
        wo = [sb(late, f"w_out_{n}", [P, DC, D], FP32R, "right") for n in ("high", "low")]
        raw = sb(late, "raw", [P, 2, 4 * HALF], FP32, "right")
        attn_side.close()
        heads_raw = sb(late, "heads_raw", [P, DC, HALF], FP32)
        hs = [sb(late, f"heads_{n}", [P, DC, HALF], FP32R) for n in ("high", "low")]
        x_tile = sb(late, "x_tile", [P, TT, D], FP32)
        h1 = sb(late, "h1", [P, TT, D], FP32)
        h1_keep = sb(late, "h1_keep", [P, TT, D], FP32)
        h1_t = [sb(late, f"h1_t_{n}", [P, DC, HALF], FP32R) for n in ("high", "low")]
        hid_raw = sb(late, "hid_raw", [P, 2, HALF], FP32)
        hid = [sb(late, f"hid_{n}", [P, 3, HALF], FP32R) for n in ("high", "low")]
        y_sb = sb(late, "y_sb", [P, D], FP32)
        z_sb = sb(late, "z_sb", [P, D], FP32)
        out_sb = sb(late, "out_sb", [P, 2, D], FP32)
        b_out_sb = sb(late, "b_out_sb", [P, D], FP32)
        gain = sb(late, "gain", [P, D], FP32)
        gain_one = sb(late, "gain_one", [P, 1], FP32)
        up_scale = sb(late, "up_scale", [P, HM], FP32)
        ident2 = sb(late, "ident2", [P, P], FP32)
        eps = sb(late, "eps", [P, 1], FP32)
        stats = sb(late, "stats", [P, 2, 6], FP32)
        moments = sb(late, "moments", [P, 2, 2], FP32)
        std = sb(late, "std", [P, 2, 1], FP32)
        rstd = sb(late, "rstd", [P, 2, 1], FP32)
        pa.close()
        ps_up = [pb(late, f"ps_up{i}", [P, HALF]) for i in range(2)]
        ps_down = [pb(late, f"ps_down{i}", [P, HALF]) for i in range(TT)]
        ps_attn = pb(late, "ps_attn", [P, HALF])
        ps_turn2 = pb(late, "ps_turn2", [P, HALF])

        s_c2 = sem("late_consts_loaded")
        s_c3 = sem("late_consts_ready")
        s_gain = sem("gain_ready")
        s_hl = sem("heads_loaded")
        s_hh = sem("heads_high_ready")
        s_hlo = sem("heads_low_ready")
        s_xt = [sem(f"x_tile_loaded{i}") for i in range(TT)]
        s_xb = sem("x_biased")
        s_at = sem("attn_out_ready")
        s_y = sem("y_ready")
        s_ln1 = sem("ln1_steps")
        s_sq1 = sem("ln1_std_ready")
        s_h1 = sem("h1_ready")
        s_keep = sem("h1_kept")
        s_tt = sem("h1_turned")
        s_th = sem("h1_t_high_ready")
        s_tl = sem("h1_t_low_ready")
        s_up = sem("up_done")
        s_hr = sem("hidden_ready")
        s_hdh = sem("hidden_high_ready")
        s_hdl = sem("hidden_low_ready")
        s_dn = sem("down_done")
        s_z = sem("down_copied")
        s_ln2 = sem("ln2_steps")
        s_sq2 = sem("ln2_std_ready")
        s_o = sem("out_ready")
        s_os = [sem(f"out_stored{i}") for i in range(2)]

        block = top.enter_context(nc.Block())
        A_LOOP = GROUPS - 1

        def steps(eng, run):
            first, last = Multiples(eng, 0), Multiples(eng, A_LOOP)
            run(Step(first, -2), plan(False, False, True, lead=True))
            run(Step(first, -1), plan(False, True, True))
            with eng.Fori(0, A_LOOP) as i:
                g = Multiples(eng, i)
                run(Step(g, 0), plan(True, True, True))
                run(Step(g, 1), plan(True, True, True))
            run(Step(last, 0), plan(True, True, False, 1))
            run(Step(last, 1), plan(True, False, False, 2))

        def wait_apart(eng, sem, value):
            wait(eng, sem, value)
            if not isinstance(value, int):
                eng.sem_inc(s_passed, 1)

        def chunk_plan(following):
            at = [[] for _ in range(HM + 4)]
            at[0].append(("keep", 0))
            for m in range(HM):
                at[m].append(("up", m))
                at[m + 2].append(("down", m))
            if following:
                at[0].append(("fetch", 0))
                for i in range(TT):
                    at[3 + 3 * i].append(("attn", i))
                    at[4 + 3 * i].append(("ln1", i))
                    at[HM + (i + 1) // 2].append(("turn", i))
            for i in range(TT):
                at[HM + 3].append(("ln2", i))
            return [x for slot in at for x in slot]

        LEAD = [("fetch", 0)] + [(w, i) for i in range(TT) for w in ("attn", "ln1")] + [("turn", i) for i in range(TT)]

        def chunks(eng, run):
            run(Multiples(eng, -1), LEAD)
            with eng.Fori(0, CH - 1) as i:
                run(Multiples(eng, i), chunk_plan(True))
            run(Multiples(eng, CH - 1), chunk_plan(False))

        @block.sync
        def _(sp):
            def load_x(b, n):
                c, t0, dst = raw_piece(b, n)
                if b == 1:
                    wait(sp, s_xh, n + 1)
                    wait(sp, s_xl, n + 1)
                sp.dma_start(dst, x_cols[c * P:(c + 1) * P, t0:t0 + HALF]).then_inc(s_x[n], 16)

            for s in s_st + s_os:
                sp.sem_inc(s, 16)
            for n in range(4):
                load_x(0, n)
            sp.dma_start(w_raw[:, :, :, :], w_qkv[0]).then_inc(s_wd, 16)
            sp.dma_start(bias_sb[:, :, :], b_qkv).then_inc(s_bias, 16)
            for n in range(4, 8):
                load_x(0, n)
            for n in range(8):
                load_x(1, n)

            def run(st, todo):
                mx = Step(st.g, st.off + 1)
                for what, n in todo:
                    if what == "weights" and st.slot == 0 and not (st.leading and st.off == -2):
                        grp = Step(st.g, st.off + 2).group
                        wait_apart(sp, s_wl, grp)
                        sp.dma_start(w_raw[:, :, :, :],
                                     w_qkv[bass.ds(grp, 1)].rearrange("a p c t e -> (a p) c t e")).then_inc(s_wd, 16)
                    if what == "stack":
                        wait_apart(sp, s_spill, mx.count(NC_, 4))
                        wait_apart(sp, s_lo, mx.count(4, 4))
                        wait(sp, s_vt, mx.count(2, 1))
                        for h in range(GH):
                            rows = slice(h * HD, (h + 1) * HD)
                            for quad, q_part, k_part in ((0, qk_h, qk_h), (1, qk_h, qk_l), (2, qk_l, qk_h)):
                                dst = slice(quad * HD, (quad + 1) * HD)
                                sp.dma_start(q_stack[dst, mx.slot, h, :].bitcast(FP32),
                                             q_part[rows, 0, :].bitcast(FP32)).then_inc(s_stack[h], 16)
                                sp.dma_start(k_stack[dst, mx.slot, h, :].bitcast(FP32),
                                             k_part[rows, 1, :].bitcast(FP32)).then_inc(s_stack[h], 16)
                    if what == "shift":
                        wait_apart(sp, s_mh, mx.count(1, 1))
                        wait(sp, s_ml, mx.count(1, 1))
                        for r, part in ((96, shift_h), (97, shift_l)):
                            sp.dma_start(q_stack[r:r + 1, mx.slot, :, :].rearrange("a h (i q) -> a (h i) q", q=P)
                                         .bitcast(FP32), part[:, :].bitcast(FP32)).then_inc(s_md, 16)
                    if what == "norm":
                        wait_apart(sp, s_norm, st.count(NHALF, n + 2))
                        t0 = st.batch * SEQ + n * HALF
                        sp.dma_start(heads_dram[bass.ds(st.group, 1), :, t0:t0 + HALF].rearrange("a p t -> (a p) t"),
                                     heads_sb[:, n, :]).then_inc(s_st[n], 16)
                    if what == "job":
                        if n == 0:
                            wait(sp, s_proj, NC_ * STEPS)
                            for h in range(GH):
                                wait(sp, s_stack[h], 96 * STEPS)
                        wait(sp, s_sign, 4 * (n - 1))
                        if n == 2:
                            wait(sp, s_wol, 1)
                        src = w_out if n == 0 else (up_w if n < 5 else down_w)[(n - 1) % 4]
                        sp.dma_start(raw[:, n % 2, :], src).then_inc(s_raw[n % 2], 16)

            steps(sp, run)

            sp.wait_ge(s_norm, NHALF * STEPS + 1)
            for f in range(NHALF):
                sp.wait_ge(s_st[f], 16 * STEPS + 16)
            sp.dma_start(b_out_sb[:, :], b_out.partition_broadcast(P)).then_inc(s_c2, 16)
            sp.dma_start(gain[:, :], down_s.partition_broadcast(P)).then_inc(s_c2, 16)
            sp.dma_start(gain_one[:, :], out_s.partition_broadcast(P)).then_inc(s_c2, 16)
            sp.dma_start(up_scale[:, :], up_s).then_inc(s_c2, 16)

            def run2(t, todo):
                def nt(k):
                    return t(k) + k

                for what, n in todo:
                    if what == "fetch":
                        wait_apart(sp, s_hh, nt(1))
                        wait_apart(sp, s_hlo, nt(1))
                        sp.dma_start(heads_raw[:, :, :],
                                     heads_dram[:, :, bass.ds(nt(HALF), HALF)].rearrange("c p t -> p c t")).then_inc(s_hl, 16)
                        for i in range(TT):
                            wait_apart(sp, s_y, nt(TT))
                            sp.dma_start(x_tile[:, i, :], x_rows[bass.ds(nt(HALF) + i * P, P), :]).then_inc(s_xt[i], 16)
                    if what == "ln2":
                        wait_apart(sp, s_o, t(TT) + n + 2)
                        sp.dma_start(out[bass.ds(t(HALF) + n * P, P), :], out_sb[:, n % 2, :]).then_inc(s_os[n % 2], 16)

            chunks(sp, run2)
            for i in range(2):
                sp.wait_ge(s_os[i], 16 * CH * TT // 2 + 16)

        @block.gpsimd
        def _(pool):
            nc.gpsimd.memset(ident[:, :], 0.0).then_inc(s_const, 1)
            nc.gpsimd.memset(causal[:, :], 0.0).then_inc(s_const, 1)
            nc.gpsimd.memset(ones[:, :], 1.0).then_inc(s_const, 1)
            nc.gpsimd.memset(maxes[:, :, :], NEG).then_inc(s_const, 1)
            pool.wait_ge(s_const, 4)
            nc.gpsimd.memset(k_stack[96:98, :, :, :].bitcast(FP32), 1.0).then_inc(s_const, 1)
            pool.wait_ge(s_const, 5)
            nc.gpsimd.affine_select(out=ident[:, :], in_=ident[:, :], compare_op=ALU.not_equal, fill=1.0, base=0,
                                    pattern=[[-1, P]], channel_multiplier=1).then_inc(s_const, 1)
            nc.gpsimd.affine_select(out=causal[:, HALF - P:], in_=causal[:, HALF - P:], compare_op=ALU.is_ge, fill=NEG,
                                    base=0, pattern=[[-1, P]], channel_multiplier=1).then_inc(s_const, 1)

            def split_weights(grp):
                pool.wait_ge(s_wh, grp + 1)
                nc.gpsimd.tensor_tensor(ws[1][:, :, :, :], w_raw[:, :, :, :], ws[0][:, :, :, :].bitcast(FP32),
                                        ALU.subtract).then_inc(s_wl, 1)

            def run(st, todo):
                pr = Step(st.g, st.off + 2)
                diag = 0
                for what, n in todo:
                    if what == "weights" and st.slot == 0:
                        split_weights(pr.group)
                    if what == "second_x":
                        c, t0, src = raw_piece(1, n)
                        pool.wait_ge(s_xh, 2 * DC + n + 1)
                        nc.gpsimd.tensor_tensor(xs[1][:, c, t0:t0 + HALF], src,
                                                xs[0][:, c, t0:t0 + HALF].bitcast(FP32),
                                                ALU.subtract).then_inc(s_xlp, 1)
                    if what == "spill" and n < 4:
                        t, f = PROJ[n]
                        wait(pool, s_spill, pr.count(NC_, n + 1))
                        nc.gpsimd.tensor_tensor(qk_l[:, t, f * HALF:(f + 1) * HALF], qk_full[:, :],
                                                qk_h[:, t, f * HALF:(f + 1) * HALF].bitcast(FP32),
                                                ALU.subtract).then_inc(s_lo, 1)
                    if what == "score" and n in DIAG:
                        wait_apart(pool, s_exp, st.count(NP, n + 1))
                        tile = probs[:, n % RING, 0:P]
                        nc.gpsimd.affine_select(out=tile, in_=tile, compare_op=ALU.is_ge, fill=0.0, base=0,
                                                pattern=[[1, P]], channel_multiplier=-1).then_inc(s_mask, 1)
                    if what == "sign" and n == 3:
                        wait(pool, s_sign, 4)
                        nc.gpsimd.tensor_tensor(wo[1][:, :, :], raw[:, 0, :].rearrange("p (c e) -> p c e", c=DC),
                                                wo[0][:, :, :].bitcast(FP32), ALU.subtract).then_inc(s_wol, 1)

            steps(pool, run)

            pool.wait_ge(s_norm, NHALF * STEPS + 1)
            nc.gpsimd.memset(ident2[:, :], 0.0).then_inc(s_c3, 1)
            nc.gpsimd.memset(eps[:, :], EPS).then_inc(s_c3, 1)
            pool.wait_ge(s_c3, 2)
            nc.gpsimd.affine_select(out=ident2[:, :], in_=ident2[:, :], compare_op=ALU.not_equal, fill=1.0, base=0,
                                    pattern=[[-1, P]], channel_multiplier=1).then_inc(s_c3, 1)
            pool.wait_ge(s_c2, 64)

            def run2(t, todo):
                def nt(k):
                    return t(k) + k

                for what, n in todo:
                    if what == "fetch":
                        for i in range(TT):
                            pool.wait_ge(s_xt[i], nt(16) + 16)
                            nc.gpsimd.tensor_tensor(x_tile[:, i, :], x_tile[:, i, :], b_out_sb[:, :],
                                                    ALU.add).then_inc(s_xb, 1)
                    if what == "up":
                        pool.wait_ge(s_hdh, t(HM) + n + 1)
                        if n >= 3:
                            pool.wait_ge(s_dn, t(HM) + n - 2)
                        nc.gpsimd.tensor_tensor(hid[1][:, n % 3, :], hid_raw[:, n % 2, :],
                                                hid[0][:, n % 3, :].bitcast(FP32), ALU.subtract).then_inc(s_hdl, 1)

            chunks(pool, run2)

        @block.scalar
        def _(act):
            def x_high(b, n):
                c, t0, src = raw_piece(b, n)
                act.wait_ge(s_x[n], 16 * (b + 1))
                nc.scalar.activation(xs[0][:, c, t0:t0 + HALF], src, ACT.Copy).then_inc(s_xh, 1)

            for n in range(8):
                x_high(0, n)
            act.wait_ge(s_bias, 16)

            def run(st, todo):
                mx, pr = Step(st.g, st.off + 1), Step(st.g, st.off + 2)
                if st.leading and st.off == -1:
                    act.wait_ge(s_xlp, 8)
                for what, n in todo:
                    if what == "second_x":
                        x_high(1, n)
                    if what == "spill":
                        t, f = PROJ[n]
                        bias = bias_g[:, pr.slot, t:t + 1]
                        act.wait_ge(s_proj, pr.count(NC_, n + 1))
                        if n == 0:
                            for h in range(GH):
                                wait(act, s_stack[h], pr.count(96))
                            nc.scalar.activation(bias_g[:, pr.slot, :],
                                                 bias_sb[:, bass.ds(pr.group, 1), :].rearrange("p a t -> p (a t)"),
                                                 ACT.Copy).then_inc(s_bias, 1)
                            act.wait_ge(s_bias, pr.count(1, 17))
                        if t < 2:
                            wait(act, s_lo, pr.count(4, n))
                            nc.scalar.activation(qk_h[:, t, f * HALF:(f + 1) * HALF], ps_proj[:, :], ACT.Identity,
                                                 bias=bias)
                            nc.scalar.activation(qk_full[:, :], ps_proj[:, :], ACT.Identity,
                                                 bias=bias).then_inc(s_spill, 1)
                        else:
                            wait(act, s_vt, pr.count(2, -2))
                            nc.scalar.activation(v_cols[:, pr.slot, f * HALF:(f + 1) * HALF], ps_proj[:, :],
                                                 ACT.Identity, bias=bias).then_inc(s_spill, 1)
                    if what == "vturn":
                        act.wait_ge(s_vt, mx.count(2, n + 1))
                        nc.scalar.activation(v_rows[:, mx.slot, 4 * n:4 * n + 4, :],
                                             ps_turn[:, :].rearrange("p (j e) -> p j e", j=4),
                                             ACT.Copy).then_inc(s_vc, 1)
                    if what == "shift":
                        wait(act, s_md, mx.count(32))
                        act.wait_ge(s_mt, mx.count(1, 1))
                        nc.scalar.activation(shift_h[:, :], ps_turn[0:GH * QT, 0:P], ACT.Copy,
                                             scale=-1.0).then_inc(s_mh, 1)
                    if what == "score":
                        _, width, _ = piece_cols(n)
                        off = P if width == P else 0
                        act.wait_ge(s_score, st.count(NP, n + 1))
                        if n >= RING:
                            act.wait_ge(s_pv, st.count(NP, n - RING + 1))
                        nc.scalar.activation(probs[:, n % RING, 0:width], ps_score[n % 2][:, off:off + width],
                                             ACT.Exp, scale=SCALE).then_inc(s_exp, 1)
                    if what == "sign":
                        k, q = n // 4, n % 4
                        act.wait_ge(s_raw[k % 2], 16 * (k // 2 + 1))
                        src = raw[:, k % 2, q * HALF:(q + 1) * HALF]
                        if k == 0:
                            nc.scalar.activation(wo[0][:, q, :], src, ACT.Copy).then_inc(s_sign, 1)
                        elif k < 5:
                            nc.scalar.activation(up_sb[:, 4 * (k - 1) + q, :, :],
                                                 src.rearrange("p (c e) -> p c e", c=DC), ACT.Sign).then_inc(s_sign, 1)
                        else:
                            nc.scalar.activation(down_sb[:, 4 * (k - 5) + q, :], src, ACT.Sign).then_inc(s_sign, 1)

            steps(act, run)

            act.wait_ge(s_c2, 64)
            act.wait_ge(s_c3, 3)

            def run2(t, todo):
                def nt(k):
                    return t(k) + k

                for what, n in todo:
                    if what == "fetch":
                        act.wait_ge(s_hl, nt(16) + 16)
                        wait(act, s_at, nt(TT))
                        nc.scalar.activation(hs[0][:, :, :], heads_raw[:, :, :], ACT.Copy).then_inc(s_hh, 1)
                    if what == "ln1":
                        act.wait_ge(s_ln1, nt(3 * TT) + 3 * n + 2)
                        nc.scalar.activation(std[:, 0, :], moments[:, 0, 1:2], ACT.Sqrt,
                                             bias=eps[:, :]).then_inc(s_sq1, 1)
                    if what == "turn":
                        act.wait_ge(s_tt, nt(TT) + n + 1)
                        nc.scalar.activation(h1_t[0][:, :, n * P:(n + 1) * P],
                                             ps_turn2[:, :].rearrange("p (c q) -> p c q", c=DC),
                                             ACT.Copy).then_inc(s_th, 1)
                    if what == "keep":
                        act.wait_ge(s_z, t(2 * TT) + 1)
                        act.wait_ge(s_h1, t(TT) + TT)
                        nc.scalar.activation(h1_keep[:, :, :], h1[:, :, :], ACT.Copy).then_inc(s_keep, 1)
                    if what == "up":
                        act.wait_ge(s_up, t(HM) + n + 1)
                        if n >= 2:
                            act.wait_ge(s_hdl, t(HM) + n - 1)
                        nc.scalar.activation(hid_raw[:, n % 2, :], ps_up[n % 2][:, :], ACT.Relu,
                                             scale=up_scale[:, n:n + 1]).then_inc(s_hr, 1)
                    if what == "ln2":
                        act.wait_ge(s_ln2, t(3 * TT) + 3 * n + 2)
                        nc.scalar.activation(std[:, 1, :], moments[:, 1, 1:2], ACT.Sqrt,
                                             bias=eps[:, :]).then_inc(s_sq2, 1)

            chunks(act, run2)

        @block.vector
        def _(dve):
            for s in (s_norm, s_z, s_o):
                dve.sem_inc(s, 1)
            for n in range(8):
                c, t0, src = raw_piece(0, n)
                if n == 4:
                    dve.wait_ge(s_wd, 16)
                    nc.vector.tensor_copy(ws[0][:, :, :, :], w_raw[:, :, :, :]).then_inc(s_wh, 1)
                dve.wait_ge(s_xh, n + 1)
                nc.vector.tensor_tensor(xs[1][:, c, t0:t0 + HALF], src, xs[0][:, c, t0:t0 + HALF].bitcast(FP32),
                                        ALU.subtract).then_inc(s_xl, 1)
            dve.wait_ge(s_const, 7)

            def run(st, todo):
                mx, pr = Step(st.g, st.off + 1), Step(st.g, st.off + 2)
                for what, n in todo:
                    if what == "weights" and st.slot == 0 and not (st.leading and st.off == -2):
                        dve.wait_ge(s_wd, pr.count(8, 16))
                        dve.wait_ge(s_proj, pr.count(NC_))
                        nc.vector.tensor_copy(ws[0][:, :, :, :], w_raw[:, :, :, :]).then_inc(s_wh, 1)
                    if what == "max":
                        h, i, c = UNITS[n]
                        col = h * QT + i
                        wait_apart(dve, s_unit, mx.count(NU, n + 1))
                        if c == i // 4:
                            width = P * (i % 4 + 1)
                            nc.vector.tensor_tensor_reduce(ps_unit[n % 2][:, 0:width], ps_unit[n % 2][:, 0:width],
                                                           causal[:, HALF - width:], 1.0, NEG, ALU.add, ALU.max,
                                                           maxes[:, 0, col:col + 1]).then_inc(s_max, 1)
                        else:
                            nc.vector.tensor_reduce(maxes[:, 1, col:col + 1], ps_unit[n % 2][:, :], AXIS_X,
                                                    ALU.max).then_inc(s_max, 1)
                    if what == "shift":
                        dve.wait_ge(s_max, mx.count(NU, NU))
                        wait(dve, s_mt, mx.count(1))
                        nc.vector.tensor_tensor(row_max[:, :], maxes[:, 0, :], maxes[:, 1, :], ALU.max).then_inc(s_mc, 1)
                        wait(dve, s_md, mx.count(32))
                        dve.wait_ge(s_mh, mx.count(1, 1))
                        nc.vector.scalar_tensor_tensor(out=shift_l[:, :], in0=ps_turn[0:GH * QT, 0:P], scalar=-1.0,
                                                       in1=shift_h[:, :].bitcast(FP32), op0=ALU.mult,
                                                       op1=ALU.subtract).then_inc(s_ml, 1)
                    if what == "norm":
                        dve.wait_ge(s_pv, st.count(NP, NP if n else 16))
                        nc.vector.reciprocal(inv_sum[:, :], ps_sum[:, :]).then_inc(s_rc, 1)
                        dve.wait_ge(s_rc, st.count(NHALF, n + 1))
                        dve.wait_ge(s_st[n], st.count(16, 16))
                        nc.vector.tensor_tensor(heads_sb[:, n, :], ps_heads[:, :], inv_sum[:, :],
                                                ALU.mult).then_inc(s_norm, 1)

            steps(dve, run)

            dve.wait_ge(s_c2, 64)
            dve.wait_ge(s_norm, NHALF * STEPS + 1)
            nc.vector.tensor_scalar(gain[:, :], gain[:, :], gain_one[:, 0:1], None, ALU.mult).then_inc(s_gain, 1)
            dve.wait_ge(s_gain, 1)

            def layer_norm(src, dst, k, steps_done, base, sq, sq_count, done):
                nc.vector.bn_stats(stats[:, k, :], src).then_inc(steps_done, 1)
                wait_apart(dve, steps_done, base + 1)
                nc.vector.bn_aggr(moments[:, k, :], stats[:, k, :]).then_inc(steps_done, 1)
                dve.wait_ge(sq, sq_count)
                nc.vector.reciprocal(rstd[:, k, :], std[:, k, :]).then_inc(steps_done, 1)
                dve.wait_ge(steps_done, base + 3)
                nc.vector.tensor_scalar(dst, src, moments[:, k, 0:1], rstd[:, k, :], ALU.subtract,
                                        ALU.mult).then_inc(done, 1)

            def run2(t, todo):
                def nt(k):
                    return t(k) + k

                for what, n in todo:
                    if what == "fetch":
                        dve.wait_ge(s_hh, nt(1) + 1)
                        nc.vector.tensor_tensor(hs[1][:, :, :], heads_raw[:, :, :], hs[0][:, :, :].bitcast(FP32),
                                                ALU.subtract).then_inc(s_hlo, 1)
                    if what == "ln1":
                        dve.wait_ge(s_at, nt(TT) + n + 1)
                        dve.wait_ge(s_xb, nt(TT) + n + 1)
                        wait(dve, s_h1, nt(TT) + n)
                        nc.vector.tensor_tensor(y_sb[:, :], ps_attn[:, :], x_tile[:, n, :], ALU.add).then_inc(s_y, 1)
                        dve.wait_ge(s_y, nt(TT) + n + 1)
                        if n == 0:
                            wait(dve, s_keep, nt(1))
                        layer_norm(y_sb[:, :], h1[:, n, :], 0, s_ln1, nt(3 * TT) + 3 * n, s_sq1,
                                   nt(TT) + n + 1, s_h1)
                    if what == "turn":
                        dve.wait_ge(s_th, nt(TT) + n + 1)
                        nc.vector.tensor_tensor(h1_t[1][:, :, n * P:(n + 1) * P],
                                                ps_turn2[:, :].rearrange("p (c q) -> p c q", c=DC),
                                                h1_t[0][:, :, n * P:(n + 1) * P].bitcast(FP32),
                                                ALU.subtract).then_inc(s_tl, 1)
                    if what == "up":
                        dve.wait_ge(s_hr, t(HM) + n + 1)
                        if n >= 3:
                            dve.wait_ge(s_dn, t(HM) + n - 2)
                        nc.vector.tensor_copy(hid[0][:, n % 3, :], hid_raw[:, n % 2, :]).then_inc(s_hdh, 1)
                    if what == "ln2":
                        if n == 0:
                            dve.wait_ge(s_dn, t(HM) + HM)
                        dve.wait_ge(s_o, t(TT) + n + 1)
                        nc.vector.tensor_tensor(z_sb[:, :], ps_down[n][:, :], gain[:, :], ALU.mult).then_inc(s_z, 1)
                        dve.wait_ge(s_z, t(2 * TT) + 2 * n + 2)
                        if n == 0:
                            dve.wait_ge(s_keep, t(1) + 1)
                        nc.vector.tensor_tensor(z_sb[:, :], z_sb[:, :], h1_keep[:, n, :], ALU.add).then_inc(s_z, 1)
                        dve.wait_ge(s_z, t(2 * TT) + 2 * n + 3)
                        dve.wait_ge(s_os[n % 2], t(32) + 16 * (n // 2) + 16)
                        layer_norm(z_sb[:, :], out_sb[:, n % 2, :], 1, s_ln2, t(3 * TT) + 3 * n, s_sq2,
                                   t(TT) + n + 1, s_o)

            chunks(dve, run2)

        @block.tensor
        def _(pe):
            pe.wait_ge(s_const, 7)

            def run(st, todo):
                mx, pr = Step(st.g, st.off + 1), Step(st.g, st.off + 2)
                diag = 0
                for what, n in todo:
                    if what == "proj":
                        k, m = n // 12, n % 12
                        t, f = PROJ[k]
                        (wp, xp), c = PARTS[m // DC], m % DC
                        t0 = pr.batch * SEQ + f * HALF
                        if n == 0 and pr.slot == 0:
                            pe.wait_ge(s_wl, pr.group + 1)
                        if st.leading and k in (0, 2):
                            sems = (s_xh, s_xl) if pr.batch == 0 else (s_xh, s_xlp)
                            if m < DC:
                                pe.wait_ge(s_xh, 8 * pr.batch + 4 * f + c + 1)
                            if m >= 2 * DC:
                                pe.wait_ge(sems[1], 4 * f + c + 1)
                        if m == 0 and k >= 1:
                            pe.wait_ge(s_spill, pr.count(NC_, k))
                        mm = nc.tensor.matmul(ps_proj[:, :], ws[wp][:, c, t, :], xs[xp][:, c, t0:t0 + HALF],
                                              start=(m == 0), stop=(m == 11))
                        if m == 11:
                            mm.then_inc(s_proj, 1)
                    if what == "vturn":
                        pe.wait_ge(s_spill, mx.count(NC_, 5 + n))
                        if n == 0:
                            wait(pe, s_ml, mx.count(1))
                        else:
                            pe.wait_ge(s_vc, mx.count(2, 1))
                        for j in range(4):
                            mm = nc.tensor.transpose(ps_turn[:, j * P:(j + 1) * P],
                                                     v_cols[:, mx.slot, (4 * n + j) * P:(4 * n + j + 1) * P],
                                                     ident[:, :])
                        mm.then_inc(s_vt, 1)
                    if what == "max":
                        h, i, c = UNITS[n]
                        width = P * (i % 4 + 1) if c == i // 4 else HALF
                        if n == 0 or UNITS[n - 1][0] != h:
                            pe.wait_ge(s_stack[h], mx.count(96, 96))
                        if n >= 2:
                            pe.wait_ge(s_max, mx.count(NU, n - 1))
                        nc.tensor.matmul(ps_unit[n % 2][:, 0:width], q_stack[0:96, mx.slot, h, i * P:(i + 1) * P],
                                         k_stack[0:96, mx.slot, h, c * HALF:c * HALF + width],
                                         start=True, stop=True).then_inc(s_unit, 1)
                    if what == "shift":
                        pe.wait_ge(s_mc, mx.count(1, 1))
                        pe.wait_ge(s_vc, mx.count(2, 2))
                        nc.tensor.transpose(ps_turn[0:GH * QT, 0:P], row_max[:, :], ident[:, :]).then_inc(s_mt, 1)
                    if what == "score":
                        f, j, h = PIECES[n]
                        lo, width, _ = piece_cols(n)
                        off = P if width == P else 0
                        if n == 0:
                            pe.wait_ge(s_md, st.count(32, 32))
                        if n >= 2:
                            pe.wait_ge(s_exp, st.count(NP, n - 1))
                        nc.tensor.matmul(ps_score[n % 2][:, 0:width + off],
                                         k_stack[0:98, st.slot, h, j * P:(j + 1) * P],
                                         q_stack[0:98, st.slot, h, lo - off:lo + width],
                                         start=True, stop=True).then_inc(s_score, 1)
                    if what == "pv":
                        f, j, h = PIECES[n]
                        _, width, at = piece_cols(n)
                        rows = slice(h * HD, (h + 1) * HD)
                        if j == 0 and h == 0:
                            pe.wait_ge(s_norm, st.count(NHALF, f + 1))
                        if n in DIAG:
                            diag += 1
                            pe.wait_ge(s_mask, st.count(ND, diag))
                        else:
                            pe.wait_ge(s_exp, st.count(NP, n + 1))
                        last = j == 4 * f + 3
                        nc.tensor.matmul(ps_heads[rows, at:at + width], v_rows[:, st.slot, j, rows],
                                         probs[:, n % RING, 0:width], start=(j == 0), stop=last,
                                         tile_position=(0, h * HD))
                        nc.tensor.matmul(ps_sum[rows, at:at + width], ones[:, :], probs[:, n % RING, 0:width],
                                         start=(j == 0), stop=last, tile_position=(0, h * HD)).then_inc(s_pv, 1)

            steps(pe, run)

            pe.wait_ge(s_sign, 4 * NJOBS)
            pe.wait_ge(s_wol, 1)
            pe.wait_ge(s_c3, 3)

            def run2(t, todo):
                def nt(k):
                    return t(k) + k

                for what, n in todo:
                    if what == "attn":
                        if n == 0:
                            pe.wait_ge(s_hlo, nt(1) + 1)
                        wait(pe, s_y, nt(TT) + n)
                        for m in range(3 * DC):
                            (wp, xp), c = PARTS[m // DC], m % DC
                            mm = nc.tensor.matmul(ps_attn[:, :], hs[xp][:, c, n * P:(n + 1) * P], wo[wp][:, c, :],
                                                  start=(m == 0), stop=(m == 3 * DC - 1))
                        mm.then_inc(s_at, 1)
                    if what == "turn":
                        pe.wait_ge(s_h1, nt(TT) + n + 1)
                        wait(pe, s_tl, nt(TT) + n)
                        for c in range(DC):
                            mm = nc.tensor.transpose(ps_turn2[:, c * P:(c + 1) * P], h1[:, n, c * P:(c + 1) * P],
                                                     ident2[:, :])
                        mm.then_inc(s_tt, 1)
                    if what == "up":
                        if n == 0:
                            pe.wait_ge(s_tl, t(TT) + TT)
                        if n >= 2:
                            pe.wait_ge(s_hr, t(HM) + n - 1)
                        for m in range(2 * DC):
                            mm = nc.tensor.matmul(ps_up[n % 2][:, :], up_sb[:, n, m % DC, :], h1_t[m // DC][:, m % DC, :],
                                                  start=(m == 0), stop=(m == 2 * DC - 1))
                        mm.then_inc(s_up, 1)
                    if what == "down":
                        pe.wait_ge(s_hdl, t(HM) + n + 1)
                        if n == 0:
                            pe.wait_ge(s_z, t(2 * TT) + 1)
                        for i in range(TT):
                            for part in range(2):
                                mm = nc.tensor.matmul(ps_down[i][:, :], hid[part][:, n % 3, i * P:(i + 1) * P],
                                                      down_sb[:, n, :], start=(n == 0 and part == 0),
                                                      stop=(n == HM - 1 and part == 1))
                        mm.then_inc(s_dn, 1)

            chunks(pe, run2)


def kernel(L0_attn_x, L0_attn_w_qkv, L0_attn_b_qkv, L0_attn_w_out, L0_attn_b_out, L0_ffn_up_weight,
           L0_ffn_down_weight, L0_ffn_up_scale, L0_ffn_down_scale, L0_ffn_output_scale):
    import concourse.bacc as bacc
    from concourse.bass_utils import run_bass_kernel_spmd

    x = np.asarray(L0_attn_x).reshape(TOKENS, D)
    arrays = {
        "x_rows": x,
        "x_cols": x.T,
        "w_qkv": np.asarray(L0_attn_w_qkv).reshape(3, GROUPS, P, DC, P).transpose(1, 4, 3, 0, 2),
        "b_qkv": np.asarray(L0_attn_b_qkv).reshape(3, GROUPS, P).transpose(2, 1, 0),
        "w_out": np.asarray(L0_attn_w_out).reshape(D, DC, P).transpose(2, 1, 0).reshape(P, DC * D),
        "b_out": np.asarray(L0_attn_b_out),
        "up_w": np.asarray(L0_ffn_up_weight).reshape(4, 4, P, DC, P).transpose(0, 4, 1, 3, 2).reshape(4, P, 4 * HALF),
        "down_w": np.asarray(L0_ffn_down_weight).reshape(D, 4, 4, P).transpose(1, 3, 2, 0).reshape(4, P, 4 * HALF),
        "up_s": np.asarray(L0_ffn_up_scale).reshape(HM, P).T,
        "down_s": np.asarray(L0_ffn_down_scale),
        "out_s": np.asarray(L0_ffn_output_scale),
    }
    arrays = {name: np.ascontiguousarray(a) for name, a in arrays.items()}
    nc = bacc.Bacc("TRN2", target_bir_lowering=False, num_devices=1)
    nc.disable_value_cache = True
    args = [nc.dram_tensor(name, a.shape, FP32, kind="ExternalInput").ap() for name, a in arrays.items()]
    out = nc.dram_tensor("out", (TOKENS, D), FP32, kind="ExternalOutput").ap()
    build(nc, *args, out)
    got = run_bass_kernel_spmd(nc, [arrays], core_ids=[0])
    return got.results[0]["out"].reshape(BATCH, SEQ, D)
```

```python
import numpy as np
import concourse.bass as bass
from concourse import mybir
from contextlib import ExitStack

FP32 = mybir.dt.float32
FP32R = mybir.dt.float32r
BF16 = mybir.dt.bfloat16
ALU = mybir.AluOpType
ACT = mybir.ActivationFunctionType
AXIS_X = mybir.AxisListType.X

P = 128
BATCH, SEQ, D, HEADS, FF = 2, 1024, 512, 16, 2048
HD = D // HEADS
TOKENS = BATCH * SEQ
DC = D // P
GROUPS = D // P
GH = P // HD
HALF = 512
NHALF = SEQ // HALF
QT = SEQ // P
STEPS = BATCH * GROUPS
SCALE = float(HD) ** -0.5
NEG = -3.0e38
EPS = 1e-5

PIECES = [(f, j, h) for f in range(NHALF) for j in range(4 * (f + 1)) for h in range(GH)]
NP = len(PIECES)
RING = 8
DIAG = [n for n, (f, j, h) in enumerate(PIECES) if j >= 4 * f]
ND = len(DIAG)
UNITS = [(h, i, c) for h in range(GH) for i in range(QT) for c in range(i // 4 + 1)]
NU = len(UNITS)
NC_ = 6
PROJ = [(0, 0), (1, 0), (0, 1), (1, 1), (2, 0), (2, 1)]
PARTS = [(0, 0), (1, 0), (0, 1)]
NJOBS = 9
CH = TOKENS // HALF
TT = HALF // P
HM = FF // P


class Multiples:

    def __init__(self, eng, i):
        self.eng, self.i, self.kept = eng, i, {}

    def __call__(self, k):
        if isinstance(self.i, int) or k == 1:
            return self.i * k
        if k not in self.kept:
            self.kept[k] = self.eng.snap(self.i * k)
        return self.kept[k]


class Step:

    def __init__(self, g, off):
        self.g, self.off, self.slot = g, off, off % 2
        self.batch, self.group = off % 2, g(1) + off // 2
        self.leading = isinstance(g(1), int) and g(1) == 0

    def count(self, per, more=0):
        return self.g(2 * per) + (self.off * per + more)


def wait(eng, sem, value):
    if not isinstance(value, int) or value > 0:
        eng.wait_ge(sem, value)


def piece_cols(n):
    f, j, _ = PIECES[n]
    lo = max(HALF * f, P * j)
    return lo, HALF * (f + 1) - lo, lo - HALF * f


PV_LAG = 6
SLOTS = NP - GH + PV_LAG + 2


def plan(attend, maxima, project, prep=0, lead=False):
    at = [[] for _ in range(SLOTS)]
    if attend:
        for n in range(NP):
            at[n].append(("score", n))
        for g in range(NP // GH):
            at[GH * g + PV_LAG].append(("pv", g))
            at[GH * g + PV_LAG + 1].append(("sum", g))
            f, j, _ = PIECES[GH * g]
            if j == 4 * f + 3:
                for q in range(4):
                    at[min(GH * g + PV_LAG + 1 + q // 2, SLOTS - 1)].append(("norm", 4 * f + q))
    if maxima:
        at[0].append(("vturn", 0))
        at[4 if attend else 1].append(("vturn", 1))
        first, last = (4, 42) if attend else (0, 30)
        for u in range(NU):
            at[first + u * (last - first) // NU].append(("max", u))
        at[last + 2].append(("shift", 0))
    if project:
        at[0].insert(0, ("load_w", 0))
        for c in range(DC):
            at[(10 if attend else 6) + c].append(("split_w", c))
        first, width = (12, 5.3) if attend else (2 if maxima else 10, 5.0)
        for k in range(NC_):
            for m in range(12):
                at[int(first + width * k + m * 0.38)].append(("proj", 12 * k + m))
            at[int(first + width * k + 11 * 0.38)].append(("spill", k))
        at[NP].append(("stack", 0))
    if lead:
        for n in range(2 * DC):
            at[12 + 4 * n].append(("second_x", n))
    if prep == 2:
        at[2].append(("early_fetch", 0))
        at[28].append(("early_split", 0))
    if prep:
        for k in (range(0, 4) if prep == 1 else range(4, NJOBS)):
            s = 8 * k + 8 if prep == 1 else 8 * (k - 4)
            at[s].append(("job", k))
            for q in range(4):
                at[s + 6 + 2 * q].append(("sign", 4 * k + q))
    return [x for slot in at for x in slot]


def build(nc, x_rows, x_cols, w_qkv, b_qkv, w_out, b_out, up_w, down_w, up_s, down_s, out_s, out):
    top = ExitStack()
    with top:
        def sem(name):
            return top.enter_context(nc.semaphore(name))

        def sb(ctx, name, shape, dt, side=None):
            return ctx.enter_context(nc.sbuf_tensor(name, shape, dt, side=side))

        def pb(ctx, name, shape):
            return ctx.enter_context(nc.psum_tensor(name, shape, FP32))

        heads_dram = nc.dram_tensor("heads_t", [GROUPS, P, TOKENS], FP32, kind="Internal").ap()

        s_const = sem("consts_ready")
        s_passed = sem("register_wait_passed")
        s_x = [sem(f"x_loaded{i}") for i in range(RING)]
        s_xh = sem("x_high_ready")
        s_xl = sem("x_low_ready")
        s_xlp = sem("x_low_ready_pool")
        s_wd = sem("w_group_loaded")
        s_bias = sem("bias_loaded")
        s_wh = sem("w_high_ready")
        s_wl = sem("w_low_ready")
        s_proj = sem("projection_done")
        s_spill = sem("projection_copied")
        s_qk = sem("qk_high_ready")
        s_lo = sem("qk_low_ready")
        s_stack = [sem(f"stack_filled{h}") for h in range(GH)]
        s_vt = sem("v_turned")
        s_vc = sem("v_ready")
        s_unit = sem("unit_scores_ready")
        s_max = sem("unit_max_ready")
        s_mc = sem("row_max_ready")
        s_mt = sem("row_max_turned")
        s_mh = sem("shift_high_ready")
        s_ml = sem("shift_low_ready")
        s_md = sem("shift_rows_filled")
        s_score = sem("scores_ready")
        s_exp = sem("probs_ready")
        s_mask = sem("probs_masked")
        s_pv = sem("probs_used")
        s_rc = sem("row_sum_inverted")
        s_norm = sem("heads_normalized")
        s_st = [sem(f"heads_stored{f}") for f in range(NHALF)]
        s_raw = [sem(f"raw_weights_loaded{i}") for i in range(2)]
        s_sign = sem("late_weights_ready")
        s_wol = sem("w_out_low_ready")

        left, right = ExitStack(), ExitStack()
        stack = sb(left, "stack", [P, 2, 2, GH, SEQ], FP32R)
        v_cols = sb(left, "v_cols", [P, 2, SEQ], FP32)
        v_rows = sb(left, "v_rows", [P, 2, QT, P], FP32)
        probs = sb(left, "probs", [P, RING, HALF], FP32)
        inv_sum = sb(left, "inv_sum", [P, HALF], FP32)
        heads_sb = sb(left, "heads_sb", [P, NHALF, HALF], FP32)
        causal = sb(left, "causal", [P, HALF], BF16)
        ident = sb(left, "ident", [P, P], FP32)
        ones = sb(left, "ones", [P, HD], FP32)
        maxes = sb(left, "maxes", [P, 2, GH * QT], FP32)
        row_max = sb(left, "row_max", [P, GH * QT], FP32)
        shift_h = sb(left, "shift_h", [GH * QT, P], FP32R)
        shift_l = sb(left, "shift_l", [GH * QT, P], FP32R)
        bias_sb = sb(left, "bias_sb", [P, GROUPS, 3], FP32)
        bias_g = sb(left, "bias_g", [P, 2, 3], FP32)

        xs = [sb(right, f"x_{n}", [P, DC, TOKENS], FP32R, "right") for n in ("high", "low")]
        w_raw = sb(right, "w_raw", [P, DC, 3, P], FP32, "right")
        ws = [sb(right, f"w_{n}", [P, DC, 3, P], FP32R, "right") for n in ("high", "low")]
        parts = sb(right, "parts", [P, 4, SEQ], FP32R, "right")
        qk_full = sb(right, "qk_full", [P, HALF], FP32, "right")

        pa = ExitStack()
        ps_proj = pb(pa, "ps_proj", [P, HALF])
        ps_turn = ps_proj
        ps_unit = [pb(pa, f"ps_unit{i}", [P, HALF]) for i in range(3)]
        ps_score = [pb(pa, f"ps_score{i}", [P, HALF]) for i in range(2)]
        ps_heads = pb(pa, "ps_heads", [P, HALF])
        ps_sum = pb(pa, "ps_sum", [P, HALF])

        def proj_bank(st, k):
            return ps_heads if st.leading and k % 2 else ps_proj

        def raw_piece(b, n):
            f, c = n // DC, n % DC
            return c, b * SEQ + f * HALF, probs[:, n, :]

        x_side, attn_side = right, left
        x_side.close()
        late = top.enter_context(ExitStack())
        up_sb = sb(late, "up_sb", [P, HM, DC, P], FP32R, "right")
        down_sb = sb(late, "down_sb", [P, HM, D], FP32R, "right")
        wo = [sb(late, f"w_out_{n}", [P, DC, D], FP32R, "right") for n in ("high", "low")]
        raw = sb(late, "raw", [P, 2, 4 * HALF], FP32, "right")
        b_out_sb = sb(late, "b_out_sb", [P, D], FP32, "right")
        gain = sb(late, "gain", [P, D], FP32, "right")
        gain_one = sb(late, "gain_one", [P, 1], FP32, "right")
        up_scale = sb(late, "up_scale", [P, HM], FP32, "right")
        ident2 = sb(late, "ident2", [P, P], FP32, "right")
        eps = sb(late, "eps", [P, 1], FP32, "right")
        attn_side.close()
        heads_raw = sb(late, "heads_raw", [P, DC, HALF], FP32)
        hs = [sb(late, f"heads_{n}", [P, DC, HALF], FP32R) for n in ("high", "low")]
        x_tile = sb(late, "x_tile", [P, TT, D], FP32)
        h1 = sb(late, "h1", [P, TT, D], FP32)
        h1_keep = sb(late, "h1_keep", [P, TT, D], FP32)
        h1_t = [sb(late, f"h1_t_{n}", [P, DC, HALF], FP32R) for n in ("high", "low")]
        hid_raw = sb(late, "hid_raw", [P, 2, HALF], FP32)
        hid = [sb(late, f"hid_{n}", [P, 3, HALF], FP32R) for n in ("high", "low")]
        y_sb = sb(late, "y_sb", [P, D], FP32)
        z_sb = sb(late, "z_sb", [P, TT, D], FP32)
        out_sb = sb(late, "out_sb", [P, 2, D], FP32)
        stats = sb(late, "stats", [P, 2, 6], FP32)
        moments = sb(late, "moments", [P, 2, 2], FP32)
        std = sb(late, "std", [P, 2, 1], FP32)
        rstd = sb(late, "rstd", [P, 2, 1], FP32)
        pa.close()
        ps_attn = pb(late, "ps_attn", [P, HALF])
        ps_turn2 = pb(late, "ps_turn2", [P, HALF])
        ps_up = [pb(late, f"ps_up{i}", [P, HALF]) for i in range(2)]
        ps_down = [pb(late, f"ps_down{i}", [P, HALF]) for i in range(TT)]

        def turn_bank(i):
            return ps_attn if i % 2 else ps_turn2

        s_c2 = sem("late_consts_loaded")
        s_c3 = sem("late_consts_ready")
        s_gain = sem("gain_ready")
        s_hl = sem("heads_loaded")
        s_hh = sem("heads_high_ready")
        s_hlo = sem("heads_low_ready")
        s_xt = [sem(f"x_tile_loaded{i}") for i in range(TT)]
        s_xb = sem("x_biased")
        s_at = sem("attn_out_ready")
        s_y = sem("y_ready")
        s_ln1 = sem("ln1_steps")
        s_sq1 = sem("ln1_std_ready")
        s_h1 = sem("h1_ready")
        s_keep = sem("h1_kept")
        s_tt = sem("h1_turned")
        s_th = sem("h1_t_high_ready")
        s_tl = sem("h1_t_low_ready")
        s_up = sem("up_done")
        s_hr = sem("hidden_ready")
        s_hdh = sem("hidden_high_ready")
        s_hdl = sem("hidden_low_ready")
        s_dn = sem("down_done")
        s_z = sem("down_copied")
        s_ln2 = sem("ln2_steps")
        s_sq2 = sem("ln2_std_ready")
        s_o = sem("out_ready")
        s_os = [sem(f"out_stored{i}") for i in range(2)]

        block = top.enter_context(nc.Block())
        A_LOOP = GROUPS - 1

        def steps(eng, run):
            first, last = Multiples(eng, 0), Multiples(eng, A_LOOP)
            run(Step(first, -2), plan(False, False, True, lead=True))
            run(Step(first, -1), plan(False, True, True))
            with eng.Fori(0, A_LOOP) as i:
                g = Multiples(eng, i)
                run(Step(g, 0), plan(True, True, True))
                run(Step(g, 1), plan(True, True, True))
            run(Step(last, 0), plan(True, True, False, 1))
            run(Step(last, 1), plan(True, False, False, 2))

        def wait_apart(eng, sem, value):
            wait(eng, sem, value)
            if not isinstance(value, int):
                eng.sem_inc(s_passed, 1)

        def chunk_plan(before, following):
            at = [[] for _ in range(HM + 4)]
            for m in range(HM):
                at[m].append(("up", m))
                at[m + 2].append(("down", m))
            if before:
                for i in range(TT):
                    at[1 + i // 2].append(("ln2", i))
            at[3].append(("keep", 0))
            if following:
                at[0].append(("fetch", 0))
                for i in range(TT):
                    at[3 + 3 * i].append(("attn", i))
                    at[4 + 3 * i].append(("ln1", i))
                at[HM] = [("turn", 0), ("turn", 1)] + at[HM] + [("turn", 2), ("turn", 3)]
            at[HM + 3].append(("z", 0))
            return [x for slot in at for x in slot]

        LEAD = [(w, i) for i in range(TT) for w in ("attn", "ln1")] + [("turn", i) for i in range(TT)]

        def chunks(eng, run):
            run(Multiples(eng, -1), LEAD)
            run(Multiples(eng, 0), chunk_plan(False, True))
            with eng.Fori(1, CH - 1) as i:
                run(Multiples(eng, i), chunk_plan(True, True))
            run(Multiples(eng, CH - 1), chunk_plan(True, False))
            run(Multiples(eng, CH), [("ln2", i) for i in range(TT)])

        @block.sync
        def _(sp):
            def load_x(b, n):
                c, t0, dst = raw_piece(b, n)
                if b == 1:
                    wait(sp, s_xh, n + 1)
                    wait(sp, s_xl, n + 1)
                sp.dma_start(dst, x_cols[c * P:(c + 1) * P, t0:t0 + HALF]).then_inc(s_x[n], 16)

            for s in s_st + s_os:
                sp.sem_inc(s, 16)
            sp.dma_start(w_raw[:, :, :, :], w_qkv[0]).then_inc(s_wd, 16)
            for n in range(4):
                load_x(0, n)
            sp.dma_start(bias_sb[:, :, :], b_qkv).then_inc(s_bias, 16)
            for n in range(4, 8):
                load_x(0, n)
            for n in range(8):
                load_x(1, n)

            def fetch(nt):
                wait_apart(sp, s_hh, nt(1))
                wait_apart(sp, s_hlo, nt(1))
                sp.dma_start(heads_raw[:, :, :],
                             heads_dram[:, :, bass.ds(nt(HALF), HALF)].rearrange("c p t -> p c t")).then_inc(s_hl, 16)
                for i in range(TT):
                    wait_apart(sp, s_y, nt(TT))
                    sp.dma_start(x_tile[:, i, :], x_rows[bass.ds(nt(HALF) + i * P, P), :]).then_inc(s_xt[i], 16)

            def run(st, todo):
                mx, pr = Step(st.g, st.off + 1), Step(st.g, st.off + 2)
                for what, n in todo:
                    if what == "early_fetch":
                        sp.wait_ge(s_score, NP * (STEPS - 1))
                        sp.wait_ge(s_st[0], 16 * (STEPS - 1) + 16)
                        fetch(lambda k: 0)
                    if what == "load_w" and st.slot == 0 and not (st.leading and st.off == -2):
                        grp = pr.group
                        wait_apart(sp, s_wl, pr.count(DC // 2))
                        sp.dma_start(w_raw[:, :, :, :],
                                     w_qkv[bass.ds(grp, 1)].rearrange("a p c t e -> (a p) c t e")).then_inc(s_wd, 16)
                    if what == "stack":
                        wait_apart(sp, s_qk, pr.count(4, 4))
                        wait_apart(sp, s_lo, pr.count(4, 4))
                        if not st.leading:
                            wait_apart(sp, s_score, st.count(NP, NP))
                        for h in range(GH):
                            rows = slice(h * HD, (h + 1) * HD)
                            for quad, pair in enumerate((slice(0, 3, 2), slice(1, 3), slice(0, 4, 3))):
                                sp.dma_start(stack[quad * HD:(quad + 1) * HD, pr.slot, :, h, :].bitcast(FP32),
                                             parts[rows, pair, :].bitcast(FP32)).then_inc(s_stack[h], 16)
                    if what == "shift":
                        wait_apart(sp, s_mh, mx.count(1, 1))
                        wait(sp, s_ml, mx.count(1, 1))
                        for r, part in ((96, shift_h), (97, shift_l)):
                            sp.dma_start(stack[r:r + 1, mx.slot, 1, :, :].rearrange("a h (i q) -> a (h i) q", q=P)
                                         .bitcast(FP32), part[:, :].bitcast(FP32)).then_inc(s_md, 16)
                    if what == "norm" and n % 4 == 3:
                        f = n // 4
                        wait_apart(sp, s_norm, st.count(QT, n + 2))
                        t0 = st.batch * SEQ + f * HALF
                        sp.dma_start(heads_dram[bass.ds(st.group, 1), :, t0:t0 + HALF].rearrange("a p t -> (a p) t"),
                                     heads_sb[:, f, :]).then_inc(s_st[f], 16)
                    if what == "job":
                        if n == 0:
                            wait(sp, s_proj, NC_ * STEPS)
                            for h in range(GH):
                                wait(sp, s_stack[h], 3 * 16 * STEPS)
                            sp.dma_start(b_out_sb[:, :], b_out.partition_broadcast(P)).then_inc(s_c2, 16)
                            sp.dma_start(gain[:, :], down_s.partition_broadcast(P)).then_inc(s_c2, 16)
                            sp.dma_start(gain_one[:, :], out_s.partition_broadcast(P)).then_inc(s_c2, 16)
                            sp.dma_start(up_scale[:, :], up_s).then_inc(s_c2, 16)
                        wait(sp, s_sign, 4 * (n - 1))
                        if n == 2:
                            wait(sp, s_wol, 1)
                        src = w_out if n == 0 else (up_w if n < 5 else down_w)[(n - 1) % 4]
                        sp.dma_start(raw[:, n % 2, :], src).then_inc(s_raw[n % 2], 16)

            steps(sp, run)

            sp.wait_ge(s_norm, QT * STEPS + 1)
            for f in range(NHALF):
                sp.wait_ge(s_st[f], 16 * STEPS + 16)

            def run2(t, todo):
                def nt(k):
                    return t(k) + k

                for what, n in todo:
                    if what == "fetch":
                        fetch(nt)
                    if what == "ln2":
                        wait_apart(sp, s_o, t(TT) + (n + 2 - TT))
                        sp.dma_start(out[bass.ds(t(HALF) + (n * P - HALF), P), :], out_sb[:, n % 2, :]).then_inc(s_os[n % 2], 16)

            chunks(sp, run2)
            for i in range(2):
                sp.wait_ge(s_os[i], 16 * CH * TT // 2 + 16)

        @block.gpsimd
        def _(pool):
            nc.gpsimd.memset(ident[:, :], 0.0).then_inc(s_const, 1)
            nc.gpsimd.memset(causal[:, :], 0.0).then_inc(s_const, 1)
            nc.gpsimd.memset(ones[:, :], 1.0).then_inc(s_const, 1)
            nc.gpsimd.memset(maxes[:, :, :], NEG).then_inc(s_const, 1)
            pool.wait_ge(s_const, 4)
            nc.gpsimd.memset(stack[96:98, :, 0, :, :].bitcast(FP32), 1.0).then_inc(s_const, 1)
            pool.wait_ge(s_const, 5)
            nc.gpsimd.affine_select(out=ident[:, :], in_=ident[:, :], compare_op=ALU.not_equal, fill=1.0, base=0,
                                    pattern=[[-1, P]], channel_multiplier=1).then_inc(s_const, 1)
            nc.gpsimd.affine_select(out=causal[:, HALF - P:], in_=causal[:, HALF - P:], compare_op=ALU.is_ge, fill=NEG,
                                    base=0, pattern=[[-1, P]], channel_multiplier=1).then_inc(s_const, 1)

            def add_bias(nt):
                for i in range(TT):
                    pool.wait_ge(s_xt[i], nt(16) + 16)
                    nc.gpsimd.tensor_tensor(x_tile[:, i, :], x_tile[:, i, :], b_out_sb[:, :],
                                            ALU.add).then_inc(s_xb, 1)

            def run(st, todo):
                pr = Step(st.g, st.off + 2)
                for what, n in todo:
                    if what == "split_w" and st.slot == 0:
                        pool.wait_ge(s_wh, pr.group + 1)
                        nc.gpsimd.tensor_tensor(ws[1][:, n, :, :], w_raw[:, n, :, :], ws[0][:, n, :, :].bitcast(FP32),
                                                ALU.subtract).then_inc(s_wl, 1)
                    if what == "second_x":
                        c, t0, src = raw_piece(1, n)
                        pool.wait_ge(s_xh, 2 * DC + n + 1)
                        nc.gpsimd.tensor_tensor(xs[1][:, c, t0:t0 + HALF], src,
                                                xs[0][:, c, t0:t0 + HALF].bitcast(FP32),
                                                ALU.subtract).then_inc(s_xlp, 1)
                    if what == "spill" and n < 4:
                        t, f = PROJ[n]
                        wait(pool, s_qk, pr.count(4, n + 1))
                        nc.gpsimd.tensor_tensor(parts[:, 3 - 2 * t, f * HALF:(f + 1) * HALF], qk_full[:, :],
                                                parts[:, 2 - 2 * t, f * HALF:(f + 1) * HALF].bitcast(FP32),
                                                ALU.subtract).then_inc(s_lo, 1)
                    if what == "score" and n in DIAG:
                        wait_apart(pool, s_exp, st.count(NP, n + 1))
                        tile = probs[:, n % RING, 0:P]
                        nc.gpsimd.affine_select(out=tile, in_=tile, compare_op=ALU.is_ge, fill=0.0, base=0,
                                                pattern=[[1, P]], channel_multiplier=-1).then_inc(s_mask, 1)
                    if what == "job" and n == 0:
                        pool.wait_ge(s_proj, NC_ * STEPS)
                        for h in range(GH):
                            pool.wait_ge(s_stack[h], 3 * 16 * STEPS)
                        nc.gpsimd.memset(ident2[:, :], 0.0).then_inc(s_c3, 1)
                        nc.gpsimd.memset(eps[:, :], EPS).then_inc(s_c3, 1)
                        pool.wait_ge(s_c3, 2)
                        nc.gpsimd.affine_select(out=ident2[:, :], in_=ident2[:, :], compare_op=ALU.not_equal, fill=1.0, base=0,
                                                pattern=[[-1, P]], channel_multiplier=1).then_inc(s_c3, 1)
                    if what == "early_split":
                        pool.wait_ge(s_c2, 64)
                        add_bias(lambda k: 0)
                    if what == "sign" and n == 3:
                        wait(pool, s_sign, 4)
                        nc.gpsimd.tensor_tensor(wo[1][:, :, :], raw[:, 0, :].rearrange("p (c e) -> p c e", c=DC),
                                                wo[0][:, :, :].bitcast(FP32), ALU.subtract).then_inc(s_wol, 1)

            steps(pool, run)

            pool.wait_ge(s_c2, 64)

            def run2(t, todo):
                def nt(k):
                    return t(k) + k

                for what, n in todo:
                    if what == "fetch":
                        add_bias(nt)
                    if what == "up":
                        pool.wait_ge(s_hdh, t(HM) + n + 1)
                        if n >= 3:
                            pool.wait_ge(s_dn, t(HM) + n - 2)
                        nc.gpsimd.tensor_tensor(hid[1][:, n % 3, :], hid_raw[:, n % 2, :],
                                                hid[0][:, n % 3, :].bitcast(FP32), ALU.subtract).then_inc(s_hdl, 1)

            chunks(pool, run2)

        @block.scalar
        def _(act):
            def x_high(b, n):
                c, t0, src = raw_piece(b, n)
                act.wait_ge(s_x[n], 16 * (b + 1))
                nc.scalar.activation(xs[0][:, c, t0:t0 + HALF], src, ACT.Copy).then_inc(s_xh, 1)

            for n in range(8):
                x_high(0, n)
            act.wait_ge(s_bias, 16)

            def heads_high(nt):
                act.wait_ge(s_hl, nt(16) + 16)
                wait(act, s_at, nt(TT))
                nc.scalar.activation(hs[0][:, :, :], heads_raw[:, :, :], ACT.Copy).then_inc(s_hh, 1)

            def run(st, todo):
                mx, pr = Step(st.g, st.off + 1), Step(st.g, st.off + 2)
                if st.leading and st.off == -1:
                    act.wait_ge(s_xlp, 8)
                for what, n in todo:
                    if what == "second_x":
                        x_high(1, n)
                    if what == "spill":
                        t, f = PROJ[n]
                        bank = proj_bank(st, n)
                        bias = bias_g[:, pr.slot, t:t + 1]
                        act.wait_ge(s_proj, pr.count(NC_, n + 1))
                        if n == 0:
                            for h in range(GH):
                                wait(act, s_stack[h], pr.count(3 * 16))
                            nc.scalar.activation(bias_g[:, pr.slot, :],
                                                 bias_sb[:, bass.ds(pr.group, 1), :].rearrange("p a t -> p (a t)"),
                                                 ACT.Copy).then_inc(s_bias, 1)
                            act.wait_ge(s_bias, pr.count(1, 17))
                        if t < 2:
                            wait(act, s_lo, pr.count(4, n))
                            nc.scalar.activation(qk_full[:, :], bank[:, :], ACT.Identity,
                                                 bias=bias).then_inc(s_spill, 1)
                            act.wait_ge(s_spill, pr.count(NC_, n + 1))
                            nc.scalar.activation(parts[:, 2 - 2 * t, f * HALF:(f + 1) * HALF], qk_full[:, :],
                                                 ACT.Copy).then_inc(s_qk, 1)
                        else:
                            wait(act, s_vt, pr.count(2, -2))
                            nc.scalar.activation(v_cols[:, pr.slot, f * HALF:(f + 1) * HALF], bank[:, :],
                                                 ACT.Identity, bias=bias).then_inc(s_spill, 1)
                    if what == "vturn":
                        act.wait_ge(s_vt, mx.count(2, n + 1))
                        nc.scalar.activation(v_rows[:, mx.slot, 4 * n:4 * n + 4, :],
                                             ps_turn[:, :].rearrange("p (j e) -> p j e", j=4),
                                             ACT.Copy).then_inc(s_vc, 1)
                    if what == "shift":
                        wait(act, s_md, mx.count(32))
                        act.wait_ge(s_mt, mx.count(1, 1))
                        nc.scalar.activation(shift_h[:, :], ps_turn[0:GH * QT, 0:P], ACT.Copy,
                                             scale=-1.0).then_inc(s_mh, 1)
                    if what == "score":
                        _, width, _ = piece_cols(n)
                        off = P if width == P else 0
                        act.wait_ge(s_score, st.count(NP, n + 1))
                        if n >= RING:
                            act.wait_ge(s_pv, st.count(NP, n - RING + 1))
                        nc.scalar.activation(probs[:, n % RING, 0:width], ps_score[n % 2][:, off:off + width],
                                             ACT.Exp, scale=SCALE).then_inc(s_exp, 1)
                    if what == "early_split":
                        heads_high(lambda k: 0)
                    if what == "sign":
                        k, q = n // 4, n % 4
                        act.wait_ge(s_raw[k % 2], 16 * (k // 2 + 1))
                        src = raw[:, k % 2, q * HALF:(q + 1) * HALF]
                        if k == 0:
                            nc.scalar.activation(wo[0][:, q, :], src, ACT.Copy).then_inc(s_sign, 1)
                        elif k < 5:
                            nc.scalar.activation(up_sb[:, 4 * (k - 1) + q, :, :],
                                                 src.rearrange("p (c e) -> p c e", c=DC), ACT.Sign).then_inc(s_sign, 1)
                        else:
                            nc.scalar.activation(down_sb[:, 4 * (k - 5) + q, :], src, ACT.Sign).then_inc(s_sign, 1)

            steps(act, run)

            act.wait_ge(s_c2, 64)
            act.wait_ge(s_c3, 3)

            def run2(t, todo):
                def nt(k):
                    return t(k) + k

                for what, n in todo:
                    if what == "fetch":
                        heads_high(nt)
                    if what == "ln1":
                        act.wait_ge(s_ln1, nt(3 * TT) + 3 * n + 2)
                        nc.scalar.activation(std[:, 0, :], moments[:, 0, 1:2], ACT.Sqrt,
                                             bias=eps[:, :]).then_inc(s_sq1, 1)
                    if what == "turn":
                        act.wait_ge(s_tt, nt(TT) + n + 1)
                        nc.scalar.activation(h1_t[0][:, :, n * P:(n + 1) * P],
                                             turn_bank(n)[:, :].rearrange("p (c q) -> p c q", c=DC),
                                             ACT.Copy).then_inc(s_th, 1)
                    if what == "keep":
                        act.wait_ge(s_z, t(2 * TT) + TT + 1)
                        act.wait_ge(s_h1, t(TT) + TT)
                        nc.scalar.activation(h1_keep[:, :, :], h1[:, :, :], ACT.Copy).then_inc(s_keep, 1)
                    if what == "up":
                        act.wait_ge(s_up, t(HM) + n + 1)
                        if n >= 2:
                            act.wait_ge(s_hdl, t(HM) + n - 1)
                        nc.scalar.activation(hid_raw[:, n % 2, :], ps_up[n % 2][:, :], ACT.Relu,
                                             scale=up_scale[:, n:n + 1]).then_inc(s_hr, 1)
                    if what == "ln2":
                        act.wait_ge(s_ln2, t(3 * TT) + (3 * n + 2 - 3 * TT))
                        nc.scalar.activation(std[:, 1, :], moments[:, 1, 1:2], ACT.Sqrt,
                                             bias=eps[:, :]).then_inc(s_sq2, 1)

            chunks(act, run2)

        @block.vector
        def _(dve):
            for s in (s_norm, s_o):
                dve.sem_inc(s, 1)
            dve.sem_inc(s_z, TT + 1)
            for n in range(8):
                c, t0, src = raw_piece(0, n)
                if n == 0:
                    dve.wait_ge(s_wd, 16)
                    nc.vector.tensor_copy(ws[0][:, :, :, :], w_raw[:, :, :, :]).then_inc(s_wh, 1)
                dve.wait_ge(s_xh, n + 1)
                nc.vector.tensor_tensor(xs[1][:, c, t0:t0 + HALF], src, xs[0][:, c, t0:t0 + HALF].bitcast(FP32),
                                        ALU.subtract).then_inc(s_xl, 1)
            dve.wait_ge(s_const, 7)

            def heads_low(nt):
                dve.wait_ge(s_hh, nt(1) + 1)
                nc.vector.tensor_tensor(hs[1][:, :, :], heads_raw[:, :, :], hs[0][:, :, :].bitcast(FP32),
                                        ALU.subtract).then_inc(s_hlo, 1)

            def run(st, todo):
                mx, pr = Step(st.g, st.off + 1), Step(st.g, st.off + 2)
                for what, n in todo:
                    if what == "split_w" and n == 0 and st.slot == 0 and not (st.leading and st.off == -2):
                        dve.wait_ge(s_wd, pr.count(8, 16))
                        dve.wait_ge(s_proj, pr.count(NC_))
                        nc.vector.tensor_copy(ws[0][:, :, :, :], w_raw[:, :, :, :]).then_inc(s_wh, 1)
                    if what == "max":
                        h, i, c = UNITS[n]
                        col = h * QT + i
                        wait_apart(dve, s_unit, mx.count(NU, n + 1))
                        if c == i // 4:
                            width = P * (i % 4 + 1)
                            nc.vector.tensor_tensor_reduce(ps_unit[n % 3][:, 0:width], ps_unit[n % 3][:, 0:width],
                                                           causal[:, HALF - width:], 1.0, NEG, ALU.add, ALU.max,
                                                           maxes[:, 0, col:col + 1]).then_inc(s_max, 1)
                        else:
                            nc.vector.tensor_reduce(maxes[:, 1, col:col + 1], ps_unit[n % 3][:, :], AXIS_X,
                                                    ALU.max).then_inc(s_max, 1)
                    if what == "shift":
                        dve.wait_ge(s_max, mx.count(NU, NU))
                        wait(dve, s_mt, mx.count(1))
                        nc.vector.tensor_tensor(row_max[:, :], maxes[:, 0, :], maxes[:, 1, :], ALU.max).then_inc(s_mc, 1)
                        wait(dve, s_md, mx.count(32))
                        dve.wait_ge(s_mh, mx.count(1, 1))
                        nc.vector.scalar_tensor_tensor(out=shift_l[:, :], in0=ps_turn[0:GH * QT, 0:P], scalar=-1.0,
                                                       in1=shift_h[:, :].bitcast(FP32), op0=ALU.mult,
                                                       op1=ALU.subtract).then_inc(s_ml, 1)
                    if what == "norm":
                        f, q = n // 4, n % 4
                        cols = slice(q * P, (q + 1) * P)
                        dve.wait_ge(s_pv, st.count(NP, NP if f else 4 * GH))
                        if q == 0:
                            dve.wait_ge(s_norm, st.count(QT, n + 1))
                        nc.vector.reciprocal(inv_sum[:, cols], ps_sum[:, cols]).then_inc(s_rc, 1)
                        dve.wait_ge(s_rc, st.count(QT, n + 1))
                        if q == 0:
                            dve.wait_ge(s_st[f], st.count(16, 16))
                        nc.vector.tensor_tensor(heads_sb[:, f, cols], ps_heads[:, cols], inv_sum[:, cols],
                                                ALU.mult).then_inc(s_norm, 1)
                    if what == "early_split":
                        heads_low(lambda k: 0)

            steps(dve, run)

            dve.wait_ge(s_c2, 64)
            dve.wait_ge(s_norm, QT * STEPS + 1)
            nc.vector.tensor_scalar(gain[:, :], gain[:, :], gain_one[:, 0:1], None, ALU.mult).then_inc(s_gain, 1)
            dve.wait_ge(s_gain, 1)

            def layer_norm(src, dst, k, steps_done, base, sq, sq_count, done):
                nc.vector.bn_stats(stats[:, k, :], src).then_inc(steps_done, 1)
                wait_apart(dve, steps_done, base + 1)
                nc.vector.bn_aggr(moments[:, k, :], stats[:, k, :]).then_inc(steps_done, 1)
                dve.wait_ge(sq, sq_count)
                nc.vector.reciprocal(rstd[:, k, :], std[:, k, :]).then_inc(steps_done, 1)
                dve.wait_ge(steps_done, base + 3)
                nc.vector.tensor_scalar(dst, src, moments[:, k, 0:1], rstd[:, k, :], ALU.subtract,
                                        ALU.mult).then_inc(done, 1)

            def run2(t, todo):
                def nt(k):
                    return t(k) + k

                for what, n in todo:
                    if what == "fetch":
                        heads_low(nt)
                    if what == "ln1":
                        dve.wait_ge(s_at, nt(TT) + n + 1)
                        dve.wait_ge(s_xb, nt(TT) + n + 1)
                        wait(dve, s_h1, nt(TT) + n)
                        nc.vector.tensor_tensor(y_sb[:, :], ps_attn[:, :], x_tile[:, n, :], ALU.add).then_inc(s_y, 1)
                        dve.wait_ge(s_y, nt(TT) + n + 1)
                        if n == 0:
                            wait(dve, s_keep, nt(1))
                        layer_norm(y_sb[:, :], h1[:, n, :], 0, s_ln1, nt(3 * TT) + 3 * n, s_sq1,
                                   nt(TT) + n + 1, s_h1)
                    if what == "turn":
                        dve.wait_ge(s_th, nt(TT) + n + 1)
                        nc.vector.tensor_tensor(h1_t[1][:, :, n * P:(n + 1) * P],
                                                turn_bank(n)[:, :].rearrange("p (c q) -> p c q", c=DC),
                                                h1_t[0][:, :, n * P:(n + 1) * P].bitcast(FP32),
                                                ALU.subtract).then_inc(s_tl, 1)
                    if what == "up":
                        dve.wait_ge(s_hr, t(HM) + n + 1)
                        if n >= 3:
                            dve.wait_ge(s_dn, t(HM) + n - 2)
                        nc.vector.tensor_copy(hid[0][:, n % 3, :], hid_raw[:, n % 2, :]).then_inc(s_hdh, 1)
                    if what == "z":
                        dve.wait_ge(s_dn, t(HM) + HM)
                        dve.wait_ge(s_o, t(TT) + 1)
                        for i in range(TT):
                            nc.vector.tensor_tensor(z_sb[:, i, :], ps_down[i][:, :], gain[:, :],
                                                    ALU.mult).then_inc(s_z, 1)
                    if what == "ln2":
                        if n == 0:
                            dve.wait_ge(s_z, t(2 * TT) + 1)
                            dve.wait_ge(s_keep, t(1))
                        nc.vector.tensor_tensor(z_sb[:, n, :], z_sb[:, n, :], h1_keep[:, n, :], ALU.add).then_inc(s_z, 1)
                        dve.wait_ge(s_z, t(2 * TT) + (n + 2))
                        dve.wait_ge(s_o, t(TT) + (n + 1 - TT))
                        dve.wait_ge(s_os[n % 2], t(32) + (16 * (n // 2) - 16))
                        layer_norm(z_sb[:, n, :], out_sb[:, n % 2, :], 1, s_ln2, t(3 * TT) + (3 * n - 3 * TT), s_sq2,
                                   t(TT) + (n + 1 - TT), s_o)

            chunks(dve, run2)

        @block.tensor
        def _(pe):
            pe.wait_ge(s_const, 7)

            def run(st, todo):
                mx, pr = Step(st.g, st.off + 1), Step(st.g, st.off + 2)
                for what, n in todo:
                    if what == "proj":
                        k, m = n // 12, n % 12
                        t, f = PROJ[k]
                        (wp, xp), c = PARTS[m // DC], m % DC
                        t0 = pr.batch * SEQ + f * HALF
                        if n == 0 and pr.slot == 0:
                            pe.wait_ge(s_wh, pr.group + 1)
                        if n in range(DC, 2 * DC) and pr.slot == 0:
                            pe.wait_ge(s_wl, pr.count(DC // 2, c + 1))
                        if st.leading and k in (0, 2):
                            sems = (s_xh, s_xl) if pr.batch == 0 else (s_xh, s_xlp)
                            if m < DC:
                                pe.wait_ge(s_xh, 8 * pr.batch + 4 * f + c + 1)
                            if m >= 2 * DC:
                                pe.wait_ge(sems[1], 4 * f + c + 1)
                        if n == 0 and not (st.leading and st.off == -2):
                            pe.wait_ge(s_vc, mx.count(2, 2))
                        if m == 0 and k >= (2 if st.leading else 1):
                            pe.wait_ge(s_spill, pr.count(NC_, k - 1 if st.leading else k))
                        mm = nc.tensor.matmul(proj_bank(st, k)[:, :], ws[wp][:, c, t, :], xs[xp][:, c, t0:t0 + HALF],
                                              start=(m == 0), stop=(m == 11))
                        if m == 11:
                            mm.then_inc(s_proj, 1)
                    if what == "vturn":
                        pe.wait_ge(s_spill, mx.count(NC_, 5 + n))
                        if n == 0:
                            wait(pe, s_ml, mx.count(1))
                        else:
                            pe.wait_ge(s_vc, mx.count(2, 1))
                        for j in range(4):
                            mm = nc.tensor.transpose(ps_turn[:, j * P:(j + 1) * P],
                                                     v_cols[:, mx.slot, (4 * n + j) * P:(4 * n + j + 1) * P],
                                                     ident[:, :])
                        mm.then_inc(s_vt, 1)
                    if what == "max":
                        h, i, c = UNITS[n]
                        width = P * (i % 4 + 1) if c == i // 4 else HALF
                        if n == 0 or UNITS[n - 1][0] != h:
                            pe.wait_ge(s_stack[h], mx.count(3 * 16, 3 * 16))
                        if n >= 3:
                            pe.wait_ge(s_max, mx.count(NU, n - 2))
                        nc.tensor.matmul(ps_unit[n % 3][:, 0:width], stack[0:96, mx.slot, 1, h, i * P:(i + 1) * P],
                                         stack[0:96, mx.slot, 0, h, c * HALF:c * HALF + width],
                                         start=True, stop=True).then_inc(s_unit, 1)
                    if what == "shift":
                        pe.wait_ge(s_mc, mx.count(1, 1))
                        pe.wait_ge(s_vc, mx.count(2, 2))
                        if ("spill", NC_ - 1) in todo:
                            pe.wait_ge(s_spill, pr.count(NC_, NC_))
                        nc.tensor.transpose(ps_turn[0:GH * QT, 0:P], row_max[:, :], ident[:, :]).then_inc(s_mt, 1)
                    if what == "score":
                        f, j, h = PIECES[n]
                        lo, width, _ = piece_cols(n)
                        off = P if width == P else 0
                        if n == 0:
                            pe.wait_ge(s_md, st.count(32, 32))
                        if n >= 2:
                            pe.wait_ge(s_exp, st.count(NP, n - 1))
                        nc.tensor.matmul(ps_score[n % 2][:, 0:width + off],
                                         stack[0:98, st.slot, 0, h, j * P:(j + 1) * P],
                                         stack[0:98, st.slot, 1, h, lo - off:lo + width],
                                         start=True, stop=True).then_inc(s_score, 1)
                    if what in ("pv", "sum"):
                        f, j, _ = PIECES[GH * n]
                        _, width, at = piece_cols(GH * n)
                        if what == "pv" and j == 0:
                            pe.wait_ge(s_norm, st.count(QT, 4 * f + 1))
                        for h in range(GH):
                            k = GH * n + h
                            rows = slice(h * HD, (h + 1) * HD)
                            args = dict(start=(j == 0), stop=(j == 4 * f + 3), tile_position=(0, h * HD))
                            if what == "sum":
                                nc.tensor.matmul(ps_sum[rows, at:at + width], ones[:, :], probs[:, k % RING, 0:width],
                                                 **args).then_inc(s_pv, 1)
                                continue
                            if k in DIAG:
                                pe.wait_ge(s_mask, st.count(ND, DIAG.index(k) + 1))
                            else:
                                pe.wait_ge(s_exp, st.count(NP, k + 1))
                            nc.tensor.matmul(ps_heads[rows, at:at + width], v_rows[:, st.slot, j, rows],
                                             probs[:, k % RING, 0:width], **args)

            steps(pe, run)

            pe.wait_ge(s_sign, 4 * NJOBS)
            pe.wait_ge(s_wol, 1)
            pe.wait_ge(s_c3, 3)

            def run2(t, todo):
                def nt(k):
                    return t(k) + k

                for what, n in todo:
                    if what == "attn":
                        if n == 0:
                            pe.wait_ge(s_hlo, nt(1) + 1)
                        wait(pe, s_y, nt(TT) + n)
                        for m in range(3 * DC):
                            (wp, xp), c = PARTS[m // DC], m % DC
                            mm = nc.tensor.matmul(ps_attn[:, :], hs[xp][:, c, n * P:(n + 1) * P], wo[wp][:, c, :],
                                                  start=(m == 0), stop=(m == 3 * DC - 1))
                        mm.then_inc(s_at, 1)
                    if what == "turn":
                        pe.wait_ge(s_h1, nt(TT) + n + 1)
                        if n == 0:
                            wait(pe, s_tl, nt(TT))
                        elif n == 1:
                            pe.wait_ge(s_y, nt(TT) + TT)
                        else:
                            pe.wait_ge(s_tl, nt(TT) + n - 1)
                        for c in range(DC):
                            mm = nc.tensor.transpose(turn_bank(n)[:, c * P:(c + 1) * P], h1[:, n, c * P:(c + 1) * P],
                                                     ident2[:, :])
                        mm.then_inc(s_tt, 1)
                    if what == "up":
                        if n == 0:
                            pe.wait_ge(s_tl, t(TT) + TT)
                        if n >= 2:
                            pe.wait_ge(s_hr, t(HM) + n - 1)
                        for m in range(2 * DC):
                            mm = nc.tensor.matmul(ps_up[n % 2][:, :], up_sb[:, n, m % DC, :], h1_t[m // DC][:, m % DC, :],
                                                  start=(m == 0), stop=(m == 2 * DC - 1))
                        mm.then_inc(s_up, 1)
                    if what == "down":
                        pe.wait_ge(s_hdl, t(HM) + n + 1)
                        if n == 0:
                            pe.wait_ge(s_z, t(2 * TT) + 1)
                        for i in range(TT):
                            for part in range(2):
                                mm = nc.tensor.matmul(ps_down[i][:, :], hid[part][:, n % 3, i * P:(i + 1) * P],
                                                      down_sb[:, n, :], start=(n == 0 and part == 0),
                                                      stop=(n == HM - 1 and part == 1))
                        mm.then_inc(s_dn, 1)

            chunks(pe, run2)


def kernel(L0_attn_x, L0_attn_w_qkv, L0_attn_b_qkv, L0_attn_w_out, L0_attn_b_out, L0_ffn_up_weight,
           L0_ffn_down_weight, L0_ffn_up_scale, L0_ffn_down_scale, L0_ffn_output_scale):
    import concourse.bacc as bacc
    from concourse.bass_utils import run_bass_kernel_spmd

    x = np.asarray(L0_attn_x).reshape(TOKENS, D)
    arrays = {
        "x_rows": x,
        "x_cols": x.T,
        "w_qkv": np.asarray(L0_attn_w_qkv).reshape(3, GROUPS, P, DC, P).transpose(1, 4, 3, 0, 2),
        "b_qkv": np.asarray(L0_attn_b_qkv).reshape(3, GROUPS, P).transpose(2, 1, 0),
        "w_out": np.asarray(L0_attn_w_out).reshape(D, DC, P).transpose(2, 1, 0).reshape(P, DC * D),
        "b_out": np.asarray(L0_attn_b_out),
        "up_w": np.asarray(L0_ffn_up_weight).reshape(4, 4, P, DC, P).transpose(0, 4, 1, 3, 2).reshape(4, P, 4 * HALF),
        "down_w": np.asarray(L0_ffn_down_weight).reshape(D, 4, 4, P).transpose(1, 3, 2, 0).reshape(4, P, 4 * HALF),
        "up_s": np.asarray(L0_ffn_up_scale).reshape(HM, P).T,
        "down_s": np.asarray(L0_ffn_down_scale),
        "out_s": np.asarray(L0_ffn_output_scale),
    }
    arrays = {name: np.ascontiguousarray(a) for name, a in arrays.items()}
    nc = bacc.Bacc("TRN2", target_bir_lowering=False, num_devices=1)
    nc.disable_value_cache = True
    args = [nc.dram_tensor(name, a.shape, FP32, kind="ExternalInput").ap() for name, a in arrays.items()]
    out = nc.dram_tensor("out", (TOKENS, D), FP32, kind="ExternalOutput").ap()
    build(nc, *args, out)
    got = run_bass_kernel_spmd(nc, [arrays], core_ids=[0])
    return got.results[0]["out"].reshape(BATCH, SEQ, D)
```
